# Optimizing a Trainium2 kernel written in Bass

```python
import numpy as np
import jax
import jax.numpy as jnp

def _softmax(x, axis=-1):
    return jax.nn.softmax(x, axis=axis)

def _gelu(x):
    return jax.nn.gelu(x, approximate=True)

def _silu(x):
    return jax.nn.silu(x)

def _sigmoid(x):
    return jax.nn.sigmoid(x)

def _layernorm(x, axis=-1, eps=1e-05):
    m = jnp.mean(x, axis=axis, keepdims=True)
    v = jnp.var(x, axis=axis, keepdims=True)
    return (x - m) / jnp.sqrt(v + eps)

def _scatter_add(tgt, idx, src, axis=0):
    return tgt.at[idx].add(src)

def _segment_sum(src, seg, n):
    return jax.ops.segment_sum(src, seg, n)
kernel_name = 'mk_dlrm_tower_d1_rec_r8_109c0c'

def setup_inputs(seed: int=0):
    np.random.seed(seed)
    _w = jnp.asarray

    def _rec_inputs():
        import jax
        import jax.numpy as jnp
        _tk = jax.random.key(seed)
        dense_ctx = jax.random.normal(jax.random.fold_in(_tk, 190), (512, 16), jnp.float32)
        ids = jnp.stack([jax.random.randint(jax.random.fold_in(_tk, 200 + f), (512,), 0, v, jnp.int32) for f, v in enumerate([125000, 1250, 1250, 1000, 1250, 1000, 125000, 1000, 125000, 1000, 1000, 1000, 1250, 1250, 1250, 1250, 12500, 12500, 1000, 1000, 1250, 1250, 12500, 12500, 1250, 12500, 1250, 1000, 1250, 1000, 1000, 1000])], axis=1)
        tbl_0 = 0.05 * jax.random.normal(jax.random.fold_in(_tk, 500 + 0), (125000, 64), jnp.float32)
        tbl_1 = 0.05 * jax.random.normal(jax.random.fold_in(_tk, 500 + 1), (1250, 64), jnp.float32)
        tbl_2 = 0.05 * jax.random.normal(jax.random.fold_in(_tk, 500 + 2), (1250, 64), jnp.float32)
        tbl_3 = 0.05 * jax.random.normal(jax.random.fold_in(_tk, 500 + 3), (1000, 64), jnp.float32)
        tbl_4 = 0.05 * jax.random.normal(jax.random.fold_in(_tk, 500 + 4), (1250, 64), jnp.float32)
        tbl_5 = 0.05 * jax.random.normal(jax.random.fold_in(_tk, 500 + 5), (1000, 64), jnp.float32)
        tbl_6 = 0.05 * jax.random.normal(jax.random.fold_in(_tk, 500 + 6), (125000, 64), jnp.float32)
        tbl_7 = 0.05 * jax.random.normal(jax.random.fold_in(_tk, 500 + 7), (1000, 64), jnp.float32)
        tbl_8 = 0.05 * jax.random.normal(jax.random.fold_in(_tk, 500 + 8), (125000, 64), jnp.float32)
        tbl_9 = 0.05 * jax.random.normal(jax.random.fold_in(_tk, 500 + 9), (1000, 64), jnp.float32)
        tbl_10 = 0.05 * jax.random.normal(jax.random.fold_in(_tk, 500 + 10), (1000, 64), jnp.float32)
        tbl_11 = 0.05 * jax.random.normal(jax.random.fold_in(_tk, 500 + 11), (1000, 64), jnp.float32)
        tbl_12 = 0.05 * jax.random.normal(jax.random.fold_in(_tk, 500 + 12), (1250, 64), jnp.float32)
        tbl_13 = 0.05 * jax.random.normal(jax.random.fold_in(_tk, 500 + 13), (1250, 64), jnp.float32)
        tbl_14 = 0.05 * jax.random.normal(jax.random.fold_in(_tk, 500 + 14), (1250, 64), jnp.float32)
        tbl_15 = 0.05 * jax.random.normal(jax.random.fold_in(_tk, 500 + 15), (1250, 64), jnp.float32)
        tbl_16 = 0.05 * jax.random.normal(jax.random.fold_in(_tk, 500 + 16), (12500, 64), jnp.float32)
        tbl_17 = 0.05 * jax.random.normal(jax.random.fold_in(_tk, 500 + 17), (12500, 64), jnp.float32)
        tbl_18 = 0.05 * jax.random.normal(jax.random.fold_in(_tk, 500 + 18), (1000, 64), jnp.float32)
        tbl_19 = 0.05 * jax.random.normal(jax.random.fold_in(_tk, 500 + 19), (1000, 64), jnp.float32)
        tbl_20 = 0.05 * jax.random.normal(jax.random.fold_in(_tk, 500 + 20), (1250, 64), jnp.float32)
        tbl_21 = 0.05 * jax.random.normal(jax.random.fold_in(_tk, 500 + 21), (1250, 64), jnp.float32)
        tbl_22 = 0.05 * jax.random.normal(jax.random.fold_in(_tk, 500 + 22), (12500, 64), jnp.float32)
        tbl_23 = 0.05 * jax.random.normal(jax.random.fold_in(_tk, 500 + 23), (12500, 64), jnp.float32)
        tbl_24 = 0.05 * jax.random.normal(jax.random.fold_in(_tk, 500 + 24), (1250, 64), jnp.float32)
        tbl_25 = 0.05 * jax.random.normal(jax.random.fold_in(_tk, 500 + 25), (12500, 64), jnp.float32)
        tbl_26 = 0.05 * jax.random.normal(jax.random.fold_in(_tk, 500 + 26), (1250, 64), jnp.float32)
        tbl_27 = 0.05 * jax.random.normal(jax.random.fold_in(_tk, 500 + 27), (1000, 64), jnp.float32)
        tbl_28 = 0.05 * jax.random.normal(jax.random.fold_in(_tk, 500 + 28), (1250, 64), jnp.float32)
        tbl_29 = 0.05 * jax.random.normal(jax.random.fold_in(_tk, 500 + 29), (1000, 64), jnp.float32)
        tbl_30 = 0.05 * jax.random.normal(jax.random.fold_in(_tk, 500 + 30), (1000, 64), jnp.float32)
        tbl_31 = 0.05 * jax.random.normal(jax.random.fold_in(_tk, 500 + 31), (1000, 64), jnp.float32)
        _rk = jax.random.fold_in(_tk, 7)
        W_top1 = 0.0693375 * jax.random.normal(jax.random.fold_in(_tk, 801), (208, 512), jnp.float32)
        W_top2 = 0.0441942 * jax.random.normal(jax.random.fold_in(_tk, 802), (512, 256), jnp.float32)
        W_top3 = 0.0625 * jax.random.normal(jax.random.fold_in(_tk, 803), (256, 1), jnp.float32)
        b_top1 = jnp.zeros((512,), jnp.float32)
        b_top2 = jnp.zeros((256,), jnp.float32)
        return (dense_ctx, ids, tbl_0, tbl_1, tbl_2, tbl_3, tbl_4, tbl_5, tbl_6, tbl_7, tbl_8, tbl_9, tbl_10, tbl_11, tbl_12, tbl_13, tbl_14, tbl_15, tbl_16, tbl_17, tbl_18, tbl_19, tbl_20, tbl_21, tbl_22, tbl_23, tbl_24, tbl_25, tbl_26, tbl_27, tbl_28, tbl_29, tbl_30, tbl_31, W_top1, b_top1, W_top2, b_top2, W_top3)
    dense_ctx, ids, tbl_0, tbl_1, tbl_2, tbl_3, tbl_4, tbl_5, tbl_6, tbl_7, tbl_8, tbl_9, tbl_10, tbl_11, tbl_12, tbl_13, tbl_14, tbl_15, tbl_16, tbl_17, tbl_18, tbl_19, tbl_20, tbl_21, tbl_22, tbl_23, tbl_24, tbl_25, tbl_26, tbl_27, tbl_28, tbl_29, tbl_30, tbl_31, W_top1, b_top1, W_top2, b_top2, W_top3 = _rec_inputs()

    def _L0_rec_setup():
        import jax, jax.numpy as jnp
        import numpy as np
        F0 = 32
        D = 64
        B = 256

        def _cin_layer(h, h0, W, b):
            Hn = h.shape[1]
            Mn = h0.shape[1]
            Wr = W.reshape(W.shape[0], Hn, Mn)
            x = jnp.einsum('bhd,bmd,ohm->bod', h, h0, Wr) + b[None, :, None]
            return jax.nn.relu(x)
        key = jax.random.key(seed)
        k1, k2, k3 = jax.random.split(key, 3)
        inputs = jax.random.normal(k1, (B, F0, D), dtype=jnp.float32)
        W1 = jax.random.normal(k2, (128, F0 * F0), dtype=jnp.float32) * (1.0 / np.sqrt(F0 * F0))
        b1 = jnp.zeros((128,), dtype=jnp.float32)
        W2 = jax.random.normal(k3, (128, 64 * F0), dtype=jnp.float32) * (1.0 / np.sqrt(64 * F0))
        b2 = jnp.zeros((128,), dtype=jnp.float32)
        return {'inputs': inputs, 'W1': W1, 'b1': b1, 'W2': W2, 'b2': b2}
    _L0_rec_all = _L0_rec_setup()
    _L0_rec_in = {k: v for k, v in _L0_rec_all.items() if k in ('W1', 'b1', 'W2', 'b2')}
    del _L0_rec_all
    return {'dense_ctx': dense_ctx, 'ids': ids, 'tbl_0': tbl_0, 'tbl_1': tbl_1, 'tbl_2': tbl_2, 'tbl_3': tbl_3, 'tbl_4': tbl_4, 'tbl_5': tbl_5, 'tbl_6': tbl_6, 'tbl_7': tbl_7, 'tbl_8': tbl_8, 'tbl_9': tbl_9, 'tbl_10': tbl_10, 'tbl_11': tbl_11, 'tbl_12': tbl_12, 'tbl_13': tbl_13, 'tbl_14': tbl_14, 'tbl_15': tbl_15, 'tbl_16': tbl_16, 'tbl_17': tbl_17, 'tbl_18': tbl_18, 'tbl_19': tbl_19, 'tbl_20': tbl_20, 'tbl_21': tbl_21, 'tbl_22': tbl_22, 'tbl_23': tbl_23, 'tbl_24': tbl_24, 'tbl_25': tbl_25, 'tbl_26': tbl_26, 'tbl_27': tbl_27, 'tbl_28': tbl_28, 'tbl_29': tbl_29, 'tbl_30': tbl_30, 'tbl_31': tbl_31, 'W_top1': W_top1, 'b_top1': b_top1, 'W_top2': W_top2, 'b_top2': b_top2, 'W_top3': W_top3, 'L0_rec_W1': _L0_rec_in['W1'], 'L0_rec_b1': _L0_rec_in['b1'], 'L0_rec_W2': _L0_rec_in['W2'], 'L0_rec_b2': _L0_rec_in['b2']}

def reference(dense_ctx, ids, tbl_0, tbl_1, tbl_2, tbl_3, tbl_4, tbl_5, tbl_6, tbl_7, tbl_8, tbl_9, tbl_10, tbl_11, tbl_12, tbl_13, tbl_14, tbl_15, tbl_16, tbl_17, tbl_18, tbl_19, tbl_20, tbl_21, tbl_22, tbl_23, tbl_24, tbl_25, tbl_26, tbl_27, tbl_28, tbl_29, tbl_30, tbl_31, W_top1, b_top1, W_top2, b_top2, W_top3, L0_rec_W1, L0_rec_b1, L0_rec_W2, L0_rec_b2):
    import jax
    import jax.numpy as jnp

    def _L0_rec_ref(inputs, W1, b1, W2, b2):
        import jax, jax.numpy as jnp
        import numpy as np
        F0 = 32
        D = 64
        B = 256

        def _cin_layer(h, h0, W, b):
            Hn = h.shape[1]
            Mn = h0.shape[1]
            Wr = W.reshape(W.shape[0], Hn, Mn)
            x = jnp.einsum('bhd,bmd,ohm->bod', h, h0, Wr) + b[None, :, None]
            return jax.nn.relu(x)
        h0 = inputs
        x1 = _cin_layer(h0, h0, W1, b1)
        next_hidden = x1[:, :64]
        direct1 = x1[:, 64:]
        direct2 = _cin_layer(next_hidden, h0, W2, b2)
        result = jnp.concatenate([direct1, direct2], axis=1)
        return jnp.sum(result, axis=-1)
    e = jnp.stack([tbl_0[ids[:, 0]], tbl_1[ids[:, 1]], tbl_2[ids[:, 2]], tbl_3[ids[:, 3]], tbl_4[ids[:, 4]], tbl_5[ids[:, 5]], tbl_6[ids[:, 6]], tbl_7[ids[:, 7]], tbl_8[ids[:, 8]], tbl_9[ids[:, 9]], tbl_10[ids[:, 10]], tbl_11[ids[:, 11]], tbl_12[ids[:, 12]], tbl_13[ids[:, 13]], tbl_14[ids[:, 14]], tbl_15[ids[:, 15]], tbl_16[ids[:, 16]], tbl_17[ids[:, 17]], tbl_18[ids[:, 18]], tbl_19[ids[:, 19]], tbl_20[ids[:, 20]], tbl_21[ids[:, 21]], tbl_22[ids[:, 22]], tbl_23[ids[:, 23]], tbl_24[ids[:, 24]], tbl_25[ids[:, 25]], tbl_26[ids[:, 26]], tbl_27[ids[:, 27]], tbl_28[ids[:, 28]], tbl_29[ids[:, 29]], tbl_30[ids[:, 30]], tbl_31[ids[:, 31]]], axis=1)
    z = _L0_rec_ref(e, L0_rec_W1, L0_rec_b1, L0_rec_W2, L0_rec_b2)
    z = z.reshape(z.shape[0], -1)
    h = jnp.concatenate([z, dense_ctx], axis=1)
    h = jnp.maximum(h @ W_top1 + b_top1, 0.0)
    h = jnp.maximum(h @ W_top2 + b_top2, 0.0)
    y = h @ W_top3
    return y

_drawn_inputs = setup_inputs


def setup_inputs(seed=0):
    import zlib

    import numpy as np

    out = dict(_drawn_inputs(seed))
    spreads = {'b_top1': (0.0, 2.0),
     'b_top2': (0.0, 2.0),
     'L0_rec_b1': (0.0, 0.325),
     'L0_rec_b2': (0.0, 0.718)}
    factors = {'tbl_0': 8.0,
     'tbl_1': 8.0,
     'tbl_2': 8.0,
     'tbl_3': 8.0,
     'tbl_4': 8.0,
     'tbl_5': 8.0,
     'tbl_6': 8.0,
     'tbl_7': 8.0,
     'tbl_8': 8.0,
     'tbl_9': 8.0,
     'tbl_10': 8.0,
     'tbl_11': 8.0,
     'tbl_12': 8.0,
     'tbl_13': 8.0,
     'tbl_14': 8.0,
     'tbl_15': 8.0,
     'tbl_16': 8.0,
     'tbl_17': 8.0,
     'tbl_18': 8.0,
     'tbl_19': 8.0,
     'tbl_20': 8.0,
     'tbl_21': 8.0,
     'tbl_22': 8.0,
     'tbl_23': 8.0,
     'tbl_24': 8.0,
     'tbl_25': 8.0,
     'tbl_26': 8.0,
     'tbl_27': 8.0,
     'tbl_28': 8.0,
     'tbl_29': 8.0,
     'tbl_30': 8.0,
     'tbl_31': 8.0,
     'L0_rec_W1': 8.0,
     'L0_rec_W2': 8.0,
     'dense_ctx': 8.0}
    for name, (base, spread) in spreads.items():
        noise = np.random.default_rng([zlib.crc32(name.encode()), seed]).standard_normal(out[name].shape)
        drawn = base * np.exp(spread * noise) if base else spread * noise
        out[name] = jnp.asarray(drawn.astype(out[name].dtype))
    for name, factor in factors.items():
        out[name] = (out[name] * factor).astype(out[name].dtype)
    return out
```

```python
from contextlib import ExitStack

import concourse.bass as bass
from concourse import mybir

ALU = mybir.AluOpType
ACT = mybir.ActivationFunctionType
F32 = mybir.dt.float32
F32R = mybir.dt.float32r
I32 = mybir.dt.int32

P = 128
BANK = 512
B, F, D = 512, 32, 64
NC = 2
N = NC * BANK
UB = N // D
U = B // UB
Q = P // F
NG = UB // Q
T1 = 4
A_ARR, B_ARR = 4, 4
HG, MG = 64 // A_ARR, F // B_ARR
T2 = A_ARR * B_ARR
L1T = 1 + T1
PER = L1T + T2
FAR = "far"
FORM1 = (0, 1, FAR, 2, 3)
MULT1 = (0, 1, 2, FAR, 3)
RING = 8
SPLIT = (2, 5, 7, 10, 12, 14)
HRING = 3
HI = 1 + len(SPLIT)
CTX = 16
N1, N2 = 512, 256
HEAD_PARTS = (slice(0, B - 2 * UB), slice(B - 2 * UB, B))
HEAD_LOADS = 6


def build(nc, ids, offs, table, w1a, w1b, w1x, b1, w2, b2, wt1z1, wt1z2, bt1, wt2, bt2, wt3, ctxT, out):
    rows = nc.dram_tensor("rows", (U, 2 * F, N), F32, kind="Internal").ap()

    def fields(offset, dims):
        return bass.AP(rows.tensor, offset * N, [[2 * F * N, U]] + [[s * N, n] for s, n in dims] + [[1, N]])

    rep_src = fields(0, [(0, Q), (1, F)])
    roll_src = [fields(4 * t, [(1, Q), (1, F)]) for t in range(T1)]
    far_src = fields(F // 2, [(0, 3), (1, F)])
    b_src = [fields(MG * j, [(0, HG), (1, MG)]) for j in range(B_ARR)]
    store_dst = [bass.AP(rows.tensor, copy * F * N, [[2 * F * N, U], [NG * D, Q], [N, F], [1, NG * D]]) for copy in range(2)]

    ctx = ExitStack()
    with ctx:
        def sb(name, shape, dt=F32):
            return ctx.enter_context(nc.sbuf_tensor(name, shape, dt))

        def pb(name, shape):
            return ctx.enter_context(nc.psum_tensor(name, shape, F32))

        def sem(name):
            return ctx.enter_context(nc.semaphore(name))

        ids_sb = sb("ids_sb", [P, U * NG], I32)
        offs_sb = sb("offs_sb", [P, 1], I32)
        idx = sb("idx", [P, U * NG], I32)
        idx_now = sb("idx_now", [P, 2, NG], I32)
        gathered = [sb(f"gathered{g}", [P, NG * D]) for g in range(2)]

        rep = sb("rep", [P, N])
        roll = [sb(f"roll{t}", [P, N]) for t in range(T1)]
        far = sb("far", [3 * F, N])
        hb = [sb(f"hb{j}", [P, N]) for j in range(B_ARR)]
        xa = [sb(f"xa{i}", [P, N]) for i in range(A_ARR)]
        x1 = sb("x1", [P, N])
        feat1 = [sb(f"feat1_{t}", [P, N]) for t in range(T1)]
        feat2 = [sb(f"feat2_{s}", [P, N]) for s in range(RING)]
        feat_x = sb("feat_x", [3 * F, N])
        part_x = sb("part_x", [3 * F, N], F32R)
        part = [sb(f"part{s}", [P, N], F32R) for s in range(HRING)]
        rest = [sb(f"rest{s}", [P, N], F32R) for s in range(HRING)]

        w1a_sb = sb("w1a_sb", [P, T1, P])
        w1b_sb = sb("w1b_sb", [P, T1, P])
        w1_sb = sb("w1_sb", [P, T1, P])
        w1x_sb = sb("w1x_sb", [3 * F, P])
        w1x_r = sb("w1x_r", [3 * F, P], F32R)
        w2_sb = sb("w2_sb", [P, T2, P])
        w2_part = sb("w2_part", [P, T2, P], F32R)
        w2_rest = sb("w2_rest", [P, T2, P], F32R)
        b1_sb, b2_sb = sb("b1_sb", [P, 1]), sb("b2_sb", [P, 1])
        wt1z1_sb, wt1z2_sb = sb("wt1z1_sb", [P, N1]), sb("wt1z2_sb", [P, N1])
        bt1_sb = sb("bt1_sb", [P, N1 // P])
        wt2_sb = sb("wt2_sb", [P, N1 // P, N2])
        bt2_sb = sb("bt2_sb", [P, N2 // P])
        wt3_sb = sb("wt3_sb", [P, N2 // P])
        z1_now, z2_now = sb("z1_now", [P, UB]), sb("z2_now", [P, UB])
        z1, z2 = sb("z1", [P, B]), sb("z2", [P, B])
        t1 = sb("t1", [P, N1 // P, B])
        t2 = sb("t2", [P, N2 // P, B])
        y_sb = sb("y_sb", [1, B])

        x1_ps = pb("x1_ps", [P, N])
        top2_ps = x1_ps[:, 0:N2 // P * B].rearrange("p (n b) -> p n b", b=B)
        x2_ps = pb("x2_ps", [P, N])
        head_ps = pb("head_ps", [P, N1 // P, B])
        y_ps = x2_ps[0:1, 0:B]

        s_ids, s_idx, s_idx_now = sem("s_ids"), sem("s_idx"), sem("s_idx_now")
        s_gather, s_store = [[sem(f"{n}{g}") for g in range(2)] for n in ("s_gather", "s_store")]
        s_store_first = sem("s_store_first")
        s_w1, s_w2, s_bias, s_head = sem("s_w1"), sem("s_w2"), sem("s_bias"), sem("s_head")
        s_ctx = sem("s_ctx")
        s_rep, s_far = sem("s_rep"), sem("s_far")
        s_roll = [sem(f"s_roll{t}") for t in range(T1)]
        s_hb = [sem(f"s_hb{j}") for j in range(B_ARR)]
        s_xa = [sem(f"s_xa{i}") for i in range(A_ARR)]
        s_w1_ready, s_w2_part, s_w2_rest = sem("s_w1_ready"), sem("s_w2_part"), sem("s_w2_rest")
        s_feat = sem("s_feat")
        s_part = sem("s_part")
        s_rest = sem("s_rest")
        s_tile = sem("s_tile")
        s_x1, s_x2 = sem("s_x1"), sem("s_x2")
        s_z1, s_z2 = sem("s_z1"), sem("s_z2")
        s_top1, s_t1, s_top2, s_t2 = sem("s_top1"), sem("s_t1"), sem("s_top2"), sem("s_t2")
        s_y_ps, s_y, s_out = sem("s_y_ps"), sem("s_y"), sem("s_out")

        def stored(pair, g):
            return (pair + g) * 32

        def first1(turn):
            return turn * PER + L1T

        def first2(turn):
            return turn * PER + 2 * L1T

        def first_split(turn):
            return turn * HI + 1

        block = ctx.enter_context(nc.Block())

        @block.gpsimd
        def _(pool):
            def gather(u, g):
                nc.gpsimd.tensor_copy(idx_now[:, g], idx[:, bass.ds(u * NG, NG)]).then_inc(s_idx_now, 1)
                pool.wait_ge(s_idx_now, u + 1)
                pool.nop(nofuse=True)
                for n in range(NG):
                    pool.indirect_dma_start(
                        gathered[g][:, n * D:(n + 1) * D], None, table,
                        bass.IndirectOffsetOnAxis(ap=idx_now[:, g, n:n + 1], axis=0)).then_inc(s_gather[g], 16)

            def store(pair, g):
                pool.wait_ge(s_gather[g], (pair + 1) * (16 * NG))
                pool.nop(nofuse=True)
                for dst in store_dst:
                    pool.dma_start(dst[pair * 2 + g], gathered[g][:]).then_inc(s_store[g], 16)

            pool.wait_ge(s_ids, 32)
            nc.gpsimd.tensor_tensor(idx[:], ids_sb[:], offs_sb[:].to_broadcast([P, U * NG]), ALU.add).then_inc(s_idx, 1)
            pool.wait_ge(s_idx, 1)
            gather(0, 0)
            gather(1, 1)
            store(0, 1)
            pool.wait_ge(s_store_first, 32)
            gather(2, 0)
            pool.wait_ge(s_store[1], 32)
            gather(3, 1)
            for g in range(2):
                store(1, g)
            with pool.Fori(2, U // 2) as pair:
                for g in range(2):
                    pool.wait_ge(s_store[g], stored(pair - 1, g))
                    gather(pair * 2 + g, g)
                for g in range(2):
                    store(pair, g)

        @block.sync
        def _(sp):
            def load_layer1(unit, pair, g, first=False):
                if first:
                    sp.wait_ge(s_store_first, 32)
                else:
                    sp.wait_ge(s_store[g], stored(pair, g))
                    sp.nop(nofuse=True)
                sp.dma_start(rep[:], rep_src[unit]).then_inc(s_rep, 16)
                for t in range(T1):
                    sp.dma_start(roll[t][:], roll_src[t][unit]).then_inc(s_roll[t], 16)
                    if t == 1:
                        sp.dma_start(far[:], far_src[unit]).then_inc(s_far, 16)

            def load_b(unit, j):
                sp.dma_start(hb[j][:], b_src[j][unit]).then_inc(s_hb[j], 16)

            def load_a(i):
                src = x1[i:i + (HG - 1) * MG + 1:MG]
                sp.dma_start(xa[i][:], src.unsqueeze(1).to_broadcast([HG, MG, N])).then_inc(s_xa[i], 16)

            def turn(t, pair=None, g=0):
                if pair is not None:
                    sp.wait_ge(s_feat, first1(t) + L1T)
                    load_layer1(t + 2, pair, g)
                m = first2(t)
                sp.wait_ge(s_x1, t + 2)
                sp.nop(nofuse=True)
                for i in range(A_ARR - 1):
                    sp.wait_ge(s_feat, m + B_ARR * (i + 1))
                    load_a(i)
                for j in range(B_ARR):
                    sp.wait_ge(s_feat, m + T2 - B_ARR + j + 1)
                    sp.nop(nofuse=True)
                    load_b(t + 1, j)
                load_a(A_ARR - 1)

            sp.dma_start(ids_sb[:], ids).then_inc(s_ids, 16)
            sp.dma_start(offs_sb[:], offs).then_inc(s_ids, 16)
            sp.dma_start(w1a_sb[:], w1a).then_inc(s_w1, 16)
            sp.dma_start(w1b_sb[:], w1b).then_inc(s_w1, 16)
            sp.dma_start(w1x_sb[:], w1x).then_inc(s_w1, 16)
            sp.dma_start(b1_sb[:], b1).then_inc(s_bias, 16)
            sp.dma_start(b2_sb[:], b2).then_inc(s_bias, 16)
            sp.dma_start(w2_sb[:], w2).then_inc(s_w2, 16)
            sp.wait_ge(s_gather[0], 16 * NG)
            for dst in store_dst:
                sp.dma_start(dst[0], gathered[0][:]).then_inc(s_store_first, 16)
            load_layer1(0, 0, 0, first=True)
            load_b(0, 0)
            load_b(0, 1)
            sp.wait_ge(s_feat, L1T)
            load_layer1(1, 0, 1)
            sp.wait_ge(s_x1, 1)
            load_a(0)
            load_b(0, 2)
            load_b(0, 3)
            for i in range(1, A_ARR):
                load_a(i)
            for dst, src in ((wt1z1_sb, wt1z1), (wt1z2_sb, wt1z2), (bt1_sb, bt1),
                             (wt2_sb, wt2), (bt2_sb, bt2), (wt3_sb, wt3)):
                sp.dma_start(dst[:], src).then_inc(s_head, 16)
            with sp.Fori(0, U // 2 - 1) as pair:
                for g in range(2):
                    turn(pair * 2 + g, pair + 1, g)
            turn(U - 2)
            sp.wait_ge(s_y, 1)
            sp.dma_start(out.rearrange("b o -> o b"), y_sb[:]).then_inc(s_out, 16)
            sp.wait_ge(s_out, 16)

        @block.vector
        def _(dve):
            def form_rest(dst, value, rounded, n):
                dve.wait_ge(s_part, n + 1)
                nc.vector.tensor_tensor(dst, value, rounded.bitcast(F32), ALU.subtract).then_inc(s_rest, 1)

            def layer1(unit, m, split, before=None):
                dve.wait_ge(s_rep, (unit + 1) * 16)
                for n, t in enumerate(FORM1):
                    if t == FAR:
                        dve.wait_ge(s_far, (unit + 1) * 16)
                        out, a, b = feat_x[:], rep[0:3 * F], far[:]
                    else:
                        dve.wait_ge(s_roll[t], (unit + 1) * 16)
                        out, a, b = feat1[t][:], rep[:], roll[t][:]
                    if before is not None:
                        dve.wait_ge(s_tile, before + MULT1.index(t) + 1)
                    nc.vector.tensor_tensor(out, a, b, ALU.mult).then_inc(s_feat, 1)
                    if n == FORM1.index(FAR) + 1:
                        dve.wait_ge(s_feat, m + n)
                        form_rest(part_x[F:2 * F], feat_x[F:2 * F], part_x[F:2 * F], split)

            def layer2(unit, m, split, before=None):
                def rest_of(k):
                    q = SPLIT[k]
                    form_rest(rest[k % HRING][:], feat2[q % RING][:], part[k % HRING][:], split + k)

                for q in range(T2):
                    i, j = divmod(q, B_ARR)
                    if j == 0:
                        dve.wait_ge(s_xa[i], (unit + 1) * 16)
                    if i == 0:
                        dve.wait_ge(s_hb[j], (unit + 1) * 16)
                    if q >= RING:
                        dve.wait_ge(s_tile, m + q - RING + 1)
                    elif before is not None:
                        dve.wait_ge(s_tile, before + T2 + q - RING + 1)
                    nc.vector.tensor_tensor(feat2[q % RING][:], xa[i][:], hb[j][:], ALU.mult).then_inc(s_feat, 1)
                    if q - 1 in SPLIT:
                        rest_of(SPLIT.index(q - 1))

            dve.wait_ge(s_w1, 48)
            nc.vector.tensor_tensor(w1_sb[:], w1a_sb[:], w1b_sb[:], ALU.add).then_inc(s_w1_ready, 1)
            nc.vector.tensor_copy(w1x_r[:], w1x_sb[:]).then_inc(s_w1_ready, 1)
            dve.wait_ge(s_w1_ready, 2)
            nc.vector.tensor_tensor(w1x_r[2 * F:3 * F], w1x_sb[2 * F:3 * F], w1x_r[2 * F:3 * F].bitcast(F32),
                                    ALU.subtract).then_inc(s_w1_ready, 1)
            dve.wait_ge(s_w2, 16)
            nc.vector.tensor_copy(w2_part[:], w2_sb[:]).then_inc(s_w2_part, 1)
            dve.wait_ge(s_w2_part, 1)
            nc.vector.tensor_tensor(w2_rest[:], w2_sb[:], w2_part[:].bitcast(F32), ALU.subtract).then_inc(s_w2_rest, 1)
            layer1(0, 0, 0)
            layer1(1, first1(0), first_split(0), before=0)
            layer2(0, first2(0), first_split(0) + 1)
            with dve.Fori(1, U - 1) as t:
                layer1(t + 1, first1(t), first_split(t), before=first1(t - 1))
                layer2(t, first2(t), first_split(t) + 1, before=first2(t - 1))
            layer2(U - 1, first1(U - 1), first_split(U - 1), before=first2(U - 2))
            dve.wait_ge(s_y_ps, len(HEAD_PARTS))
            nc.vector.tensor_copy(y_sb[:], y_ps).then_inc(s_y, 1)

        @block.scalar
        def _(act):
            def round_x(m, before=None):
                act.wait_ge(s_feat, m + FORM1.index(FAR) + 1)
                if before is not None:
                    act.wait_ge(s_tile, before + MULT1.index(FAR) + 1)
                nc.scalar.activation(part_x[:], feat_x[:], ACT.Copy).then_inc(s_part, 1)

            def round_part(k, m, before=None):
                q = SPLIT[k]
                act.wait_ge(s_feat, m + q + 1)
                if k >= HRING:
                    act.wait_ge(s_tile, m + SPLIT[k - HRING] + 1)
                elif before is not None:
                    act.wait_ge(s_tile, before + SPLIT[k - HRING] + 1)
                nc.scalar.activation(part[k % HRING][:], feat2[q % RING][:], ACT.Copy).then_inc(s_part, 1)

            def relu_sums(samples, src, bias, dst, sums, done):
                for b in samples:
                    last = nc.scalar.activation(dst[:, b * D:(b + 1) * D], src[:, b * D:(b + 1) * D], ACT.Relu,
                                                bias=bias[:], accum_out=sums[:, b:b + 1])
                if UB - 1 in samples:
                    last.then_inc(done, 1)

            def keep(sums, kept, unit, read, done):
                act.wait_ge(read, unit + 1)
                nc.scalar.activation(kept[:, bass.ds(unit * UB, UB)], sums[:], ACT.Copy).then_inc(done, 1)

            def drain1(samples, unit, m, first=False):
                if 0 in samples:
                    act.wait_ge(s_tile, m + L1T)
                    if not first:
                        act.wait_ge(s_z1, unit)
                        for i in range(A_ARR):
                            act.wait_ge(s_xa[i], unit * 16)
                relu_sums(samples, x1_ps, b1_sb, x1, z1_now, s_x1)

            def drain2(unit, m, first=False):
                act.wait_ge(s_tile, m + T2)
                if not first:
                    act.wait_ge(s_z2, unit)
                relu_sums(range(UB), x2_ps, b2_sb, x2_ps, z2_now, s_x2)
                keep(z2_now, z2, unit, s_x2, s_z2)

            def turn(t, before1, before2=None):
                m1, m2 = first1(t), first2(t)
                round_x(m1, before1)
                if before2 is not None:
                    drain2(t - 1, before2)
                pieces = [range(UB)[UB * k // 4:UB * (k + 1) // 4] for k in range(4)]
                for k in range(len(SPLIT)):
                    round_part(k, m2, before2)
                    if k < 4:
                        drain1(pieces[k], t + 1, m1)
                keep(z1_now, z1, t + 1, s_x1, s_z1)

            def relu_top1(h):
                cols = HEAD_PARTS[h]
                for n in range(N1 // P):
                    act.wait_ge(s_top1, h * (N1 // P) + n + 1)
                    nc.scalar.activation(t1[:, n, cols], head_ps[:, n, cols], ACT.Relu,
                                         bias=bt1_sb[:, n:n + 1]).then_inc(s_t1, 1)

            def relu_top2(h):
                cols = HEAD_PARTS[h]
                for n in range(N2 // P):
                    act.wait_ge(s_top2, h * (N2 // P) + n + 1)
                    nc.scalar.activation(t2[:, n, cols], top2_ps[:, n, cols], ACT.Relu,
                                         bias=bt2_sb[:, n:n + 1]).then_inc(s_t2, 1)

            act.wait_ge(s_bias, 32)
            round_x(0)
            drain1(range(UB), 0, 0, first=True)
            keep(z1_now, z1, 0, s_x1, s_z1)
            turn(0, 0)
            with act.Fori(1, U - 1) as t:
                turn(t, first1(t - 1), first2(t - 1))
            act.wait_ge(s_z1, U)
            act.dma_start(z1[0:(CTX - 1) * MG + 1:MG], ctxT).then_inc(s_ctx, 16)
            drain2(U - 2, first2(U - 2))
            for k in range(len(SPLIT)):
                round_part(k, first1(U - 1), first2(U - 2))
            relu_top1(0)
            drain2(U - 1, first1(U - 1))
            relu_top2(0)
            relu_top1(1)
            relu_top2(1)

        @block.tensor
        def _(pe):
            def chunks(ps, w, x, start, stop):
                for c in range(NC):
                    last = nc.tensor.matmul(ps[:, c * BANK:(c + 1) * BANK], w, x[:, c * BANK:(c + 1) * BANK],
                                            start=start, stop=stop)
                return last

            def layer1(unit, m, split, first=False):
                if not first:
                    pe.wait_ge(s_x1, unit)
                for n, t in enumerate(MULT1):
                    if t == FAR:
                        pe.wait_ge(s_part, split + 1)
                        pe.wait_ge(s_rest, split + 1)
                        w, x = w1x_r[:], part_x
                    else:
                        pe.wait_ge(s_feat, m + FORM1.index(t) + 1)
                        w, x = w1_sb[:, t, :], feat1[t]
                    chunks(x1_ps, w, x, n == 0, n == L1T - 1).then_inc(s_tile, 1)

            def layer2(unit, m, split, first=False):
                if not first:
                    pe.wait_ge(s_x2, unit)
                for q in range(T2):
                    start, stop = q == 0, q == T2 - 1
                    if q in SPLIT:
                        k = SPLIT.index(q)
                        pe.wait_ge(s_part, split + k + 1)
                        chunks(x2_ps, w2_part[:, q, :], part[k % HRING], start, False)
                        chunks(x2_ps, w2_rest[:, q, :], part[k % HRING], False, False)
                        pe.wait_ge(s_rest, split + k + 1)
                        last = chunks(x2_ps, w2_part[:, q, :], rest[k % HRING], False, stop)
                    else:
                        pe.wait_ge(s_feat, m + q + 1)
                        last = chunks(x2_ps, w2_sb[:, q, :], feat2[q % RING], start, stop)
                    last.then_inc(s_tile, 1)

            pe.wait_ge(s_w1_ready, 3)
            layer1(0, 0, 0, first=True)
            layer1(1, first1(0), first_split(0))
            pe.wait_ge(s_w2_rest, 1)
            layer2(0, first2(0), first_split(0) + 1, first=True)
            with pe.Fori(1, U - 1) as t:
                layer1(t + 1, first1(t), first_split(t))
                layer2(t, first2(t), first_split(t) + 1)

            def top1(h, units):
                cols = HEAD_PARTS[h]
                pe.wait_ge(s_z2, units)
                for n in range(N1 // P):
                    w = slice(n * P, (n + 1) * P)
                    nc.tensor.matmul(head_ps[:, n, cols], wt1z1_sb[:, w], z1[:, cols], start=True, stop=False)
                    nc.tensor.matmul(head_ps[:, n, cols], wt1z2_sb[:, w], z2[:, cols],
                                     start=False, stop=True).then_inc(s_top1, 1)

            def top2(h):
                cols = HEAD_PARTS[h]
                for n in range(N2 // P):
                    for k in range(N1 // P):
                        if n == 0:
                            pe.wait_ge(s_t1, h * (N1 // P) + k + 1)
                        last = nc.tensor.matmul(top2_ps[:, n, cols], wt2_sb[:, k, n * P:(n + 1) * P],
                                                t1[:, k, cols], start=k == 0, stop=k == N1 // P - 1)
                    last.then_inc(s_top2, 1)

            def top3(h):
                cols = HEAD_PARTS[h]
                for k in range(N2 // P):
                    pe.wait_ge(s_t2, h * (N2 // P) + k + 1)
                    last = nc.tensor.matmul(y_ps[:, cols], wt3_sb[:, k:k + 1], t2[:, k, cols],
                                            start=k == 0, stop=k == N2 // P - 1)
                last.then_inc(s_y_ps, 1)

            pe.wait_ge(s_head, 16 * HEAD_LOADS)
            pe.wait_ge(s_ctx, 16)
            top1(0, U - 2)
            layer2(U - 1, first1(U - 1), first_split(U - 1))
            top2(0)
            top1(1, U)
            top3(0)
            top2(1)
            top3(1)


def kernel(**inputs):
    import numpy as np
    import concourse.bacc as bacc
    from concourse.bass_utils import run_bass_kernel_spmd

    x = {k: np.ascontiguousarray(v) for k, v in inputs.items()}
    tables = [x[f"tbl_{f}"] for f in range(F)]
    starts = np.cumsum([0] + [t.shape[0] for t in tables[:-1]]).astype(np.int32)
    f = np.arange(F)
    far = (f + F // 2) % F
    order = np.array([(r % MG % 4) * HG + r // MG + (64 if r % MG >= 4 else 0) for r in range(P)])
    w1 = x["L0_rec_W1"].reshape(P, F, F)[order]
    shift = np.arange(Q * T1).reshape(T1, Q)
    to = (f[None, None, :] + shift[:, :, None]) % F
    frm = np.broadcast_to(f, to.shape)
    w1a = w1[:, frm, to].transpose(2, 3, 1, 0).reshape(P, T1, P)
    w1b = w1[:, to, frm].transpose(2, 3, 1, 0).reshape(P, T1, P).copy()
    w1b[:F, 0] = 0.0
    w1x = np.tile(w1[:, f, far].T, (3, 1))
    w2 = x["L0_rec_W2"].reshape(P, A_ARR, HG, B_ARR, MG).transpose(2, 4, 1, 3, 0).reshape(P, T2, P)
    top1 = x["W_top1"]
    direct = order >= 64
    wt1z1 = np.zeros((P, N1), top1.dtype)
    wt1z1[direct] = top1[order[direct] - 64]
    wt1z1[0:(CTX - 1) * MG + 1:MG] = top1[64 + P:]
    arrays = {
        "ids": x["ids"].reshape(U, Q, NG, F).transpose(1, 3, 0, 2).reshape(P, U * NG),
        "offs": np.tile(starts, Q).reshape(P, 1),
        "table": np.concatenate(tables, axis=0),
        "w1a": w1a, "w1b": w1b, "w1x": w1x, "b1": x["L0_rec_b1"][order].reshape(P, 1),
        "w2": w2, "b2": x["L0_rec_b2"].reshape(P, 1),
        "wt1z1": wt1z1, "wt1z2": top1[64:64 + P], 
        "bt1": x["b_top1"].reshape(N1 // P, P).T,
        "wt2": x["W_top2"].reshape(N1 // P, P, N2).transpose(1, 0, 2),
        "bt2": x["b_top2"].reshape(N2 // P, P).T,
        "wt3": x["W_top3"].reshape(N2 // P, P).T,
        "ctxT": x["dense_ctx"].T,
    }
    nc = bacc.Bacc("TRN2", target_bir_lowering=False, num_devices=1)
    feed, aps = {}, []
    for name, a in arrays.items():
        a = np.ascontiguousarray(a)
        feed["in_" + name] = a
        aps.append(nc.dram_tensor("in_" + name, a.shape, mybir.dt.from_np(a.dtype), kind="ExternalInput").ap())
    aps.append(nc.dram_tensor("out_y", (B, 1), F32, kind="ExternalOutput").ap())
    build(nc, *aps)
    return run_bass_kernel_spmd(nc, [feed], core_ids=[0]).results[0]["out_y"]
```

```python
from collections import namedtuple
from contextlib import ExitStack

import concourse.bass as bass
from concourse import mybir

ALU = mybir.AluOpType
ACT = mybir.ActivationFunctionType
F32 = mybir.dt.float32
F32R = mybir.dt.float32r
I32 = mybir.dt.int32

P = 128
BANK = 512
B, F, D = 512, 32, 64
NC = 2
N = NC * BANK
UB = N // D
U = B // UB
Q = P // F
NG = UB // Q
T1 = 4
A_ARR, B_ARR = 4, 4
HG, MG = 64 // A_ARR, F // B_ARR
T2 = A_ARR * B_ARR
L1T = 1 + T1
PER = L1T + T2
FAR = "far"
FORM1 = ((0, 1), (FAR,), (2, 3))
MULT1 = (0, 1, 2, FAR, 3)
STEPS = len(FORM1) + T2 // 2
RING = 8
SPLIT = ((4, 5), (7,), (10, 11), (12, 13))
RESTS = (4, 5, 6, 7)
GRING = 2
HI = 1 + len(SPLIT)
CTX = 16
N1, N2 = 512, 256
HEAD_PARTS = (slice(0, B - 2 * UB), slice(B - 2 * UB, B))
HEAD_LOADS = 6


def build(nc, ids, offs, table, w1a, w1b, w1x, b1, w2, b2, wt1z1, wt1z2, bt1, wt2, bt2, wt3, ctxT, out):
    rows = nc.dram_tensor("rows", (U, 2 * F, N), F32, kind="Internal").ap()

    def fields(offset, dims):
        return bass.AP(rows.tensor, offset * N, [[2 * F * N, U]] + [[s * N, n] for s, n in dims] + [[1, N]])

    rep_src = fields(0, [(0, Q), (1, F)])
    roll_src = [fields(4 * t, [(1, Q), (1, F)]) for t in range(T1)]
    far_src = fields(F // 2, [(0, 3), (1, F)])
    b_src = [fields(MG * j, [(0, HG), (1, MG)]) for j in range(B_ARR)]
    store_dst = [bass.AP(rows.tensor, copy * F * N, [[2 * F * N, U], [NG * D, Q], [N, F], [1, NG * D]]) for copy in range(2)]

    ctx = ExitStack()
    with ctx:
        def sb(name, shape, dt=F32):
            return ctx.enter_context(nc.sbuf_tensor(name, shape, dt))

        def pb(name, shape):
            return ctx.enter_context(nc.psum_tensor(name, shape, F32))

        def sem(name):
            return ctx.enter_context(nc.semaphore(name))

        ids_sb = sb("ids_sb", [P, U * NG], I32)
        offs_sb = sb("offs_sb", [P, 1], I32)
        idx = sb("idx", [P, U * NG], I32)
        idx_now = sb("idx_now", [P, 2, NG], I32)
        gathered = [sb(f"gathered{g}", [P, NG * D]) for g in range(2)]

        rep = sb("rep", [P, N])
        roll = sb("roll", [P, T1, N])
        far = sb("far", [3 * F, N])
        hb = sb("hb", [P, B_ARR, N])
        xa = [sb(f"xa{i}", [P, N]) for i in range(A_ARR)]
        x1 = sb("x1", [P, N])
        feat1 = sb("feat1", [P, T1, N])
        feat2 = sb("feat2", [P, RING, N])
        feat_x = sb("feat_x", [3 * F, N])
        part_x = sb("part_x", [3 * F, N], F32R)
        part = sb("part", [P, GRING, 2, N], F32R)
        rest = sb("rest", [P, GRING, 2, N], F32R)

        w1_sb = sb("w1_sb", [P, T1, P])
        w1b_sb = sb("w1b_sb", [P, T1, P])
        w1x_sb = sb("w1x_sb", [3 * F, P])
        w1x_r = sb("w1x_r", [3 * F, P], F32R)
        w2_sb = sb("w2_sb", [P, T2, P])
        w2_part = sb("w2_part", [P, T2, P], F32R)
        w2_rest = sb("w2_rest", [P, T2, P], F32R)
        b1_sb, b2_sb = sb("b1_sb", [P, 1]), sb("b2_sb", [P, 1])
        wt1z1_sb, wt1z2_sb = sb("wt1z1_sb", [P, N1]), sb("wt1z2_sb", [P, N1])
        bt1_sb = sb("bt1_sb", [P, N1 // P])
        wt2_sb = sb("wt2_sb", [P, N1 // P, N2])
        bt2_sb = sb("bt2_sb", [P, N2 // P])
        wt3_sb = sb("wt3_sb", [P, N2 // P])
        z1_now, z2_now = sb("z1_now", [P, UB]), sb("z2_now", [P, UB])
        z1, z2 = sb("z1", [P, B]), sb("z2", [P, B])
        t1 = sb("t1", [P, N1 // P, B])
        t2 = sb("t2", [P, N2 // P, B])
        y_sb = sb("y_sb", [1, B])

        x1_ps = pb("x1_ps", [P, N])
        top2_ps = x1_ps[:, 0:N2 // P * B].rearrange("p (n b) -> p n b", b=B)
        x2_ps = pb("x2_ps", [P, N])
        head_ps = pb("head_ps", [P, N1 // P, B])
        y_ps = x2_ps[0:1, 0:B]

        s_ids, s_idx, s_idx_now = sem("s_ids"), sem("s_idx"), sem("s_idx_now")
        s_gather, s_store = [[sem(f"{n}{g}") for g in range(2)] for n in ("s_gather", "s_store")]
        s_store_first = sem("s_store_first")
        s_w1, s_w2, s_bias, s_head = sem("s_w1"), sem("s_w2"), sem("s_bias"), sem("s_head")
        s_ctx = sem("s_ctx")
        s_rep, s_far = sem("s_rep"), sem("s_far")
        s_roll = [sem(f"s_roll{t}") for t in range(T1)]
        s_hb = [sem(f"s_hb{j}") for j in range(B_ARR)]
        s_xa = [sem(f"s_xa{i}") for i in range(A_ARR)]
        s_w1_ready, s_w2_part, s_w2_rest = sem("s_w1_ready"), sem("s_w2_part"), sem("s_w2_rest")
        s_feat = sem("s_feat")
        s_part = sem("s_part")
        s_rest = sem("s_rest")
        s_tile = sem("s_tile")
        s_x1, s_x2 = sem("s_x1"), sem("s_x2")
        s_z1, s_z2 = sem("s_z1"), sem("s_z2")
        s_top1, s_t1, s_top2, s_t2 = sem("s_top1"), sem("s_t1"), sem("s_top2"), sem("s_t2")
        s_y_ps, s_y, s_out = sem("s_y_ps"), sem("s_y"), sem("s_out")

        def stored(pair, g):
            return (pair + g) * 32

        At = namedtuple("At", "tile step split")
        start = At(0, 0, 0)

        def at1(turn):
            return At(turn * PER + L1T, turn * STEPS + len(FORM1), turn * HI + 1)

        def at2(turn):
            return At(turn * PER + 2 * L1T, turn * STEPS + 2 * len(FORM1), turn * HI + 2)

        end = at1(U - 1)

        block = ctx.enter_context(nc.Block())

        @block.gpsimd
        def _(pool):
            def gather(u, g):
                nc.gpsimd.tensor_copy(idx_now[:, g], idx[:, bass.ds(u * NG, NG)]).then_inc(s_idx_now, 1)
                pool.wait_ge(s_idx_now, u + 1)
                pool.nop(nofuse=True)
                for n in range(NG):
                    pool.indirect_dma_start(
                        gathered[g][:, n * D:(n + 1) * D], None, table,
                        bass.IndirectOffsetOnAxis(ap=idx_now[:, g, n:n + 1], axis=0)).then_inc(s_gather[g], 16)

            def store(pair, g):
                pool.wait_ge(s_gather[g], (pair + 1) * (16 * NG))
                pool.nop(nofuse=True)
                for dst in store_dst:
                    pool.dma_start(dst[pair * 2 + g], gathered[g][:]).then_inc(s_store[g], 16)

            pool.wait_ge(s_ids, 32)
            nc.gpsimd.tensor_tensor(idx[:], ids_sb[:], offs_sb[:].to_broadcast([P, U * NG]), ALU.add).then_inc(s_idx, 1)
            pool.wait_ge(s_idx, 1)
            gather(0, 0)
            gather(1, 1)
            store(0, 1)
            pool.wait_ge(s_store_first, 32)
            gather(2, 0)
            pool.wait_ge(s_store[1], 32)
            gather(3, 1)
            for g in range(2):
                store(1, g)
            with pool.Fori(2, U // 2) as pair:
                for g in range(2):
                    pool.wait_ge(s_store[g], stored(pair - 1, g))
                    gather(pair * 2 + g, g)
                for g in range(2):
                    store(pair, g)

        @block.sync
        def _(sp):
            def load_layer1(unit, pair, g, first=False):
                if first:
                    sp.wait_ge(s_store_first, 32)
                else:
                    sp.wait_ge(s_store[g], stored(pair, g))
                    sp.nop(nofuse=True)
                sp.dma_start(rep[:], rep_src[unit]).then_inc(s_rep, 16)
                for t in range(T1):
                    sp.dma_start(roll[:, t, :], roll_src[t][unit]).then_inc(s_roll[t], 16)
                    if t == 1:
                        sp.dma_start(far[:], far_src[unit]).then_inc(s_far, 16)

            def load_b(unit, j):
                sp.dma_start(hb[:, j, :], b_src[j][unit]).then_inc(s_hb[j], 16)

            def load_a(i):
                src = x1[i:i + (HG - 1) * MG + 1:MG]
                sp.dma_start(xa[i][:], src.unsqueeze(1).to_broadcast([HG, MG, N])).then_inc(s_xa[i], 16)

            def turn(t, pair=None, g=0):
                if pair is not None:
                    sp.wait_ge(s_feat, at1(t).step + len(FORM1))
                    load_layer1(t + 2, pair, g)
                step = at2(t).step
                sp.wait_ge(s_x1, t + 2)
                sp.nop(nofuse=True)
                for i in range(A_ARR - 1):
                    sp.wait_ge(s_feat, step + B_ARR // 2 * (i + 1))
                    load_a(i)
                for j in range(B_ARR):
                    if j % 2 == 0:
                        sp.wait_ge(s_feat, step + (T2 - B_ARR + j) // 2 + 1)
                        sp.nop(nofuse=True)
                    load_b(t + 1, j)
                load_a(A_ARR - 1)

            sp.dma_start(ids_sb[:], ids).then_inc(s_ids, 16)
            sp.dma_start(offs_sb[:], offs).then_inc(s_ids, 16)
            sp.dma_start(w1_sb[:], w1a).then_inc(s_w1, 16)
            sp.dma_start(w1b_sb[:], w1b).then_inc(s_w1, 16)
            sp.dma_start(w1x_sb[:], w1x).then_inc(s_w1, 16)
            sp.dma_start(b1_sb[:], b1).then_inc(s_bias, 16)
            sp.dma_start(b2_sb[:], b2).then_inc(s_bias, 16)
            sp.dma_start(w2_sb[:], w2).then_inc(s_w2, 16)
            sp.wait_ge(s_gather[0], 16 * NG)
            for dst in store_dst:
                sp.dma_start(dst[0], gathered[0][:]).then_inc(s_store_first, 16)
            load_layer1(0, 0, 0, first=True)
            load_b(0, 0)
            load_b(0, 1)
            sp.wait_ge(s_feat, len(FORM1))
            load_layer1(1, 0, 1)
            sp.wait_ge(s_x1, 1)
            load_a(0)
            load_b(0, 2)
            load_b(0, 3)
            for i in range(1, A_ARR):
                load_a(i)
            for dst, src in ((wt1z1_sb, wt1z1), (wt1z2_sb, wt1z2), (bt1_sb, bt1),
                             (wt2_sb, wt2), (bt2_sb, bt2), (wt3_sb, wt3)):
                sp.dma_start(dst[:], src).then_inc(s_head, 16)
            with sp.Fori(0, U // 2 - 1) as pair:
                for g in range(2):
                    turn(pair * 2 + g, pair + 1, g)
            turn(U - 2)
            sp.wait_ge(s_y, 1)
            sp.dma_start(out.rearrange("b o -> o b"), y_sb[:]).then_inc(s_out, 16)
            sp.wait_ge(s_out, 16)

        @block.vector
        def _(dve):
            def form_rest(dst, value, rounded, group):
                dve.wait_ge(s_part, group + 1)
                nc.vector.tensor_tensor(dst, value, rounded.bitcast(F32), ALU.subtract).then_inc(s_rest, 1)

            def layer1(unit, at, before=None):
                dve.wait_ge(s_rep, (unit + 1) * 16)
                for n, tiles in enumerate(FORM1):
                    if tiles == (FAR,):
                        dve.wait_ge(s_far, (unit + 1) * 16)
                        out, a, b = feat_x[:], rep[0:3 * F], far[:]
                    else:
                        for t in tiles:
                            dve.wait_ge(s_roll[t], (unit + 1) * 16)
                        pair = slice(tiles[0], tiles[0] + 2)
                        out, a, b = feat1[:, pair, :], rep[:].unsqueeze(1).to_broadcast([P, 2, N]), roll[:, pair, :]
                    if before is not None:
                        dve.wait_ge(s_tile, before.tile + MULT1.index(tiles[-1]) + 1)
                    nc.vector.tensor_tensor(out, a, b, ALU.mult).then_inc(s_feat, 1)
                dve.wait_ge(s_feat, at.step + FORM1.index((FAR,)) + 1)
                form_rest(part_x[F:2 * F], feat_x[F:2 * F], part_x[F:2 * F], at.split)

            def layer2(unit, at, before=None):
                def rest_of(k):
                    q, n = SPLIT[k][0], len(SPLIT[k])
                    form_rest(rest[:, k % GRING, 0:n, :], feat2[:, q % RING:q % RING + n, :],
                              part[:, k % GRING, 0:n, :], at.split + k)

                for q in range(0, T2, 2):
                    i, j = divmod(q, B_ARR)
                    if j == 0:
                        dve.wait_ge(s_xa[i], (unit + 1) * 16)
                    if i == 0:
                        dve.wait_ge(s_hb[j], (unit + 1) * 16)
                        dve.wait_ge(s_hb[j + 1], (unit + 1) * 16)
                    if q >= RING:
                        dve.wait_ge(s_tile, at.tile + q + 1 - RING + 1)
                    elif before is not None:
                        dve.wait_ge(s_tile, before.tile + T2 + q + 1 - RING + 1)
                    slot = q % RING
                    nc.vector.tensor_tensor(feat2[:, slot:slot + 2, :], xa[i][:].unsqueeze(1).to_broadcast([P, 2, N]),
                                            hb[:, j:j + 2, :], ALU.mult).then_inc(s_feat, 1)
                    for k, after in enumerate(RESTS):
                        if after == q // 2:
                            rest_of(k)

            dve.wait_ge(s_w1, 48)
            nc.vector.tensor_tensor(w1_sb[:], w1_sb[:], w1b_sb[:], ALU.add).then_inc(s_w1_ready, 1)
            nc.vector.tensor_copy(w1x_r[:], w1x_sb[:]).then_inc(s_w1_ready, 1)
            dve.wait_ge(s_w1_ready, 2)
            nc.vector.tensor_tensor(w1x_r[2 * F:3 * F], w1x_sb[2 * F:3 * F], w1x_r[2 * F:3 * F].bitcast(F32),
                                    ALU.subtract).then_inc(s_w1_ready, 1)
            dve.wait_ge(s_w2, 16)
            nc.vector.tensor_copy(w2_part[:], w2_sb[:]).then_inc(s_w2_part, 1)
            dve.wait_ge(s_w2_part, 1)
            nc.vector.tensor_tensor(w2_rest[:], w2_sb[:], w2_part[:].bitcast(F32), ALU.subtract).then_inc(s_w2_rest, 1)
            layer1(0, start)
            layer1(1, at1(0), start)
            layer2(0, at2(0))
            with dve.Fori(1, U - 1) as t:
                layer1(t + 1, at1(t), at1(t - 1))
                layer2(t, at2(t), at2(t - 1))
            layer2(U - 1, end, at2(U - 2))
            dve.wait_ge(s_y_ps, len(HEAD_PARTS))
            nc.vector.tensor_copy(y_sb[:], y_ps).then_inc(s_y, 1)

        @block.scalar
        def _(act):
            def round_x(at, before=None):
                act.wait_ge(s_feat, at.step + FORM1.index((FAR,)) + 1)
                if before is not None:
                    act.wait_ge(s_tile, before.tile + MULT1.index(FAR) + 1)
                nc.scalar.activation(part_x[:], feat_x[:], ACT.Copy).then_inc(s_part, 1)

            def round_part(k, at, before=None):
                q, n = SPLIT[k][0], len(SPLIT[k])
                act.wait_ge(s_feat, at.step + q // 2 + 1)
                if k >= GRING:
                    act.wait_ge(s_tile, at.tile + SPLIT[k - GRING][-1] + 1)
                elif before is not None:
                    act.wait_ge(s_tile, before.tile + SPLIT[k - GRING][-1] + 1)
                nc.scalar.activation(part[:, k % GRING, 0:n, :], feat2[:, q % RING:q % RING + n, :],
                                     ACT.Copy).then_inc(s_part, 1)

            def relu_sums(samples, src, bias, dst, sums, done):
                for b in samples:
                    last = nc.scalar.activation(dst[:, b * D:(b + 1) * D], src[:, b * D:(b + 1) * D], ACT.Relu,
                                                bias=bias[:], accum_out=sums[:, b:b + 1])
                if UB - 1 in samples:
                    last.then_inc(done, 1)

            def keep(sums, kept, unit, read, done):
                act.wait_ge(read, unit + 1)
                nc.scalar.activation(kept[:, bass.ds(unit * UB, UB)], sums[:], ACT.Copy).then_inc(done, 1)

            def drain1(samples, unit, at, first=False):
                if 0 in samples:
                    act.wait_ge(s_tile, at.tile + L1T)
                    if not first:
                        act.wait_ge(s_z1, unit)
                        for i in range(A_ARR):
                            act.wait_ge(s_xa[i], unit * 16)
                relu_sums(samples, x1_ps, b1_sb, x1, z1_now, s_x1)

            def drain2(unit, at, first=False):
                act.wait_ge(s_tile, at.tile + T2)
                if not first:
                    act.wait_ge(s_z2, unit)
                relu_sums(range(UB), x2_ps, b2_sb, x2_ps, z2_now, s_x2)
                keep(z2_now, z2, unit, s_x2, s_z2)

            def turn(t, before1, before2=None):
                round_x(at1(t), before1)
                if before2 is not None:
                    drain2(t - 1, before2)
                drain1(range(8), t + 1, at1(t))
                round_part(0, at2(t), before2)
                drain1(range(8, UB), t + 1, at1(t))
                for k in range(1, len(SPLIT)):
                    round_part(k, at2(t), before2)
                keep(z1_now, z1, t + 1, s_x1, s_z1)

            def relu_top1(h):
                cols = HEAD_PARTS[h]
                for n in range(N1 // P):
                    act.wait_ge(s_top1, h * (N1 // P) + n + 1)
                    nc.scalar.activation(t1[:, n, cols], head_ps[:, n, cols], ACT.Relu,
                                         bias=bt1_sb[:, n:n + 1]).then_inc(s_t1, 1)

            def relu_top2(h):
                cols = HEAD_PARTS[h]
                for n in range(N2 // P):
                    act.wait_ge(s_top2, h * (N2 // P) + n + 1)
                    nc.scalar.activation(t2[:, n, cols], top2_ps[:, n, cols], ACT.Relu,
                                         bias=bt2_sb[:, n:n + 1]).then_inc(s_t2, 1)

            act.wait_ge(s_bias, 32)
            round_x(start)
            drain1(range(UB), 0, start, first=True)
            keep(z1_now, z1, 0, s_x1, s_z1)
            turn(0, start)
            with act.Fori(1, U - 1) as t:
                turn(t, at1(t - 1), at2(t - 1))
            act.wait_ge(s_z1, U)
            act.dma_start(z1[0:(CTX - 1) * MG + 1:MG], ctxT).then_inc(s_ctx, 16)
            drain2(U - 2, at2(U - 2))
            for k in range(len(SPLIT)):
                round_part(k, end, at2(U - 2))
            relu_top1(0)
            drain2(U - 1, end)
            relu_top2(0)
            relu_top1(1)
            relu_top2(1)

        @block.tensor
        def _(pe):
            def chunks(ps, w, x, start, stop):
                for c in range(NC):
                    last = nc.tensor.matmul(ps[:, c * BANK:(c + 1) * BANK], w, x[:, c * BANK:(c + 1) * BANK],
                                            start=start, stop=stop)
                return last

            def layer1(unit, at, first=False):
                if not first:
                    pe.wait_ge(s_x1, unit)
                for n, t in enumerate(MULT1):
                    if t == FAR:
                        pe.wait_ge(s_part, at.split + 1)
                        pe.wait_ge(s_rest, at.split + 1)
                        w, x = w1x_r[:], part_x
                    else:
                        step, = [k for k, tiles in enumerate(FORM1) if t in tiles]
                        pe.wait_ge(s_feat, at.step + step + 1)
                        w, x = w1_sb[:, t, :], feat1[:, t, :]
                    chunks(x1_ps, w, x, n == 0, n == L1T - 1).then_inc(s_tile, 1)

            def layer2(unit, at, first=False):
                if not first:
                    pe.wait_ge(s_x2, unit)
                whole = [q for q in range(T2) if not any(q in group for group in SPLIT)]
                for q in range(T2):
                    for k, group in enumerate(SPLIT):
                        if q != group[0]:
                            continue
                        pe.wait_ge(s_part, at.split + k + 1)
                        for n, g in enumerate(group):
                            chunks(x2_ps, w2_part[:, g, :], part[:, k % GRING, n, :], g == 0, False)
                            chunks(x2_ps, w2_rest[:, g, :], part[:, k % GRING, n, :], False, False)
                        pe.wait_ge(s_rest, at.split + k + 1)
                        for n, g in enumerate(group):
                            chunks(x2_ps, w2_part[:, g, :], rest[:, k % GRING, n, :],
                                   False, g == T2 - 1).then_inc(s_tile, 1)
                    if q in whole:
                        pe.wait_ge(s_feat, at.step + q // 2 + 1)
                        chunks(x2_ps, w2_sb[:, q, :], feat2[:, q % RING, :], q == 0, q == T2 - 1).then_inc(s_tile, 1)

            pe.wait_ge(s_w1_ready, 3)
            layer1(0, start, first=True)
            layer1(1, at1(0))
            pe.wait_ge(s_w2_rest, 1)
            layer2(0, at2(0), first=True)
            with pe.Fori(1, U - 1) as t:
                layer1(t + 1, at1(t))
                layer2(t, at2(t))

            def top1(h, units):
                cols = HEAD_PARTS[h]
                pe.wait_ge(s_z2, units)
                for n in range(N1 // P):
                    w = slice(n * P, (n + 1) * P)
                    nc.tensor.matmul(head_ps[:, n, cols], wt1z1_sb[:, w], z1[:, cols], start=True, stop=False)
                    nc.tensor.matmul(head_ps[:, n, cols], wt1z2_sb[:, w], z2[:, cols],
                                     start=False, stop=True).then_inc(s_top1, 1)

            def top2(h):
                cols = HEAD_PARTS[h]
                for n in range(N2 // P):
                    for k in range(N1 // P):
                        if n == 0:
                            pe.wait_ge(s_t1, h * (N1 // P) + k + 1)
                        last = nc.tensor.matmul(top2_ps[:, n, cols], wt2_sb[:, k, n * P:(n + 1) * P],
                                                t1[:, k, cols], start=k == 0, stop=k == N1 // P - 1)
                    last.then_inc(s_top2, 1)

            def top3(h):
                cols = HEAD_PARTS[h]
                for k in range(N2 // P):
                    pe.wait_ge(s_t2, h * (N2 // P) + k + 1)
                    last = nc.tensor.matmul(y_ps[:, cols], wt3_sb[:, k:k + 1], t2[:, k, cols],
                                            start=k == 0, stop=k == N2 // P - 1)
                last.then_inc(s_y_ps, 1)

            pe.wait_ge(s_head, 16 * HEAD_LOADS)
            pe.wait_ge(s_ctx, 16)
            top1(0, U - 2)
            layer2(U - 1, end)
            top2(0)
            top1(1, U)
            top3(0)
            top2(1)
            top3(1)


def kernel(**inputs):
    import numpy as np
    import concourse.bacc as bacc
    from concourse.bass_utils import run_bass_kernel_spmd

    x = {k: np.ascontiguousarray(v) for k, v in inputs.items()}
    tables = [x[f"tbl_{f}"] for f in range(F)]
    starts = np.cumsum([0] + [t.shape[0] for t in tables[:-1]]).astype(np.int32)
    f = np.arange(F)
    far = (f + F // 2) % F
    order = np.array([(r % MG % 4) * HG + r // MG + (64 if r % MG >= 4 else 0) for r in range(P)])
    w1 = x["L0_rec_W1"].reshape(P, F, F)[order]
    shift = np.arange(Q * T1).reshape(T1, Q)
    to = (f[None, None, :] + shift[:, :, None]) % F
    frm = np.broadcast_to(f, to.shape)
    w1a = w1[:, frm, to].transpose(2, 3, 1, 0).reshape(P, T1, P)
    w1b = w1[:, to, frm].transpose(2, 3, 1, 0).reshape(P, T1, P).copy()
    w1b[:F, 0] = 0.0
    w1x = np.tile(w1[:, f, far].T, (3, 1))
    w2 = x["L0_rec_W2"].reshape(P, A_ARR, HG, B_ARR, MG).transpose(2, 4, 1, 3, 0).reshape(P, T2, P)
    top1 = x["W_top1"]
    direct = order >= 64
    wt1z1 = np.zeros((P, N1), top1.dtype)
    wt1z1[direct] = top1[order[direct] - 64]
    wt1z1[0:(CTX - 1) * MG + 1:MG] = top1[64 + P:]
    arrays = {
        "ids": x["ids"].reshape(U, Q, NG, F).transpose(1, 3, 0, 2).reshape(P, U * NG),
        "offs": np.tile(starts, Q).reshape(P, 1),
        "table": np.concatenate(tables, axis=0),
        "w1a": w1a, "w1b": w1b, "w1x": w1x, "b1": x["L0_rec_b1"][order].reshape(P, 1),
        "w2": w2, "b2": x["L0_rec_b2"].reshape(P, 1),
        "wt1z1": wt1z1, "wt1z2": top1[64:64 + P], 
        "bt1": x["b_top1"].reshape(N1 // P, P).T,
        "wt2": x["W_top2"].reshape(N1 // P, P, N2).transpose(1, 0, 2),
        "bt2": x["b_top2"].reshape(N2 // P, P).T,
        "wt3": x["W_top3"].reshape(N2 // P, P).T,
        "ctxT": x["dense_ctx"].T,
    }
    nc = bacc.Bacc("TRN2", target_bir_lowering=False, num_devices=1)
    feed, aps = {}, []
    for name, a in arrays.items():
        a = np.ascontiguousarray(a)
        feed["in_" + name] = a
        aps.append(nc.dram_tensor("in_" + name, a.shape, mybir.dt.from_np(a.dtype), kind="ExternalInput").ap())
    aps.append(nc.dram_tensor("out_y", (B, 1), F32, kind="ExternalOutput").ap())
    build(nc, *aps)
    return run_bass_kernel_spmd(nc, [feed], core_ids=[0]).results[0]["out_y"]
```

```python
from collections import namedtuple
from contextlib import ExitStack

import concourse.bass as bass
from concourse import mybir

ALU = mybir.AluOpType
ACT = mybir.ActivationFunctionType
F32 = mybir.dt.float32
F32R = mybir.dt.float32r
I32 = mybir.dt.int32

P = 128
BANK = 512
B, F, D = 512, 32, 64
NC = 2
N = NC * BANK
UB = N // D
U = B // UB
Q = P // F
NG = UB // Q
T1 = 4
A_ARR, B_ARR = 4, 4
HG, MG = 64 // A_ARR, F // B_ARR
T2 = A_ARR * B_ARR
L1T = 1 + T1
PER = L1T + T2
FAR = "far"
FORM1 = ((0, 1), (FAR,), (2, 3))
MULT1 = (0, 1, 2, FAR, 3)
STEPS = len(FORM1) + T2 // 2
RING = 8
SPLIT = ((4, 5), (7,), (10, 11), (12, 13))
RESTS = (4, 5, 6, 7)
GRING = 2
HI = 1 + len(SPLIT)
XF = F // 2
XC = P // (NC * XF)
XK = 3 * XF
CTX = 16
N1, N2 = 512, 256
HEAD_LOADS = 6
HEAD_PARTS = (slice(0, B - 2 * UB), slice(B - 2 * UB, B))


def build(nc, ids, offs, table, w1a, w1b, w1x, minus, b1, w2, b2, wt1z1, wt1z2, bt1, wt2, bt2, wt3, ctxT, out):
    rows = nc.dram_tensor("rows", (U, 2 * F, N), F32, kind="Internal").ap()

    def fields(offset, dims):
        return bass.AP(rows.tensor, offset * N, [[2 * F * N, U]] + [[s * N, n] for s, n in dims] + [[1, N]])

    rep_src = fields(0, [(0, Q), (1, F)])
    roll_src = [fields(4 * t, [(1, Q), (1, F)]) for t in range(T1)]
    x_src = [[bass.AP(rows.tensor, side * XF * N + c * BANK, [[2 * F * N, U], [0, XC], [N, XF], [1, BANK]])
              for c in range(NC)] for side in range(2)]
    b_src = [fields(MG * j, [(0, HG), (1, MG)]) for j in range(B_ARR)]
    store_dst = [bass.AP(rows.tensor, copy * F * N, [[2 * F * N, U], [NG * D, Q], [N, F], [1, NG * D]]) for copy in range(2)]

    ctx = ExitStack()
    with ctx:
        def sb(name, shape, dt=F32):
            return ctx.enter_context(nc.sbuf_tensor(name, shape, dt))

        def pb(name, shape):
            return ctx.enter_context(nc.psum_tensor(name, shape, F32))

        def sem(name):
            return ctx.enter_context(nc.semaphore(name))

        ids_sb = sb("ids_sb", [P, U * NG], I32)
        offs_sb = sb("offs_sb", [P, 1], I32)
        idx = sb("idx", [P, U * NG], I32)
        idx_now = sb("idx_now", [P, 2, NG], I32)
        gathered = [sb(f"gathered{g}", [P, NG * D]) for g in range(2)]

        rep = sb("rep", [P, N])
        roll = sb("roll", [P, T1, N])
        x_sides = sb("x_sides", [P, 2, BANK])
        hb = sb("hb", [P, B_ARR, N])
        xa = [sb(f"xa{i}", [P, N]) for i in range(A_ARR)]
        x1 = sb("x1", [P, N])
        feat1 = sb("feat1", [P, T1, N])
        feat2 = sb("feat2", [P, RING, N])
        feat_x = sb("feat_x", [P, BANK])
        part_x = sb("part_x", [P, BANK], F32R)
        split_x = sb("split_x", [P, BANK], F32R)
        part = sb("part", [P, GRING, 2, N], F32R)
        rest = sb("rest", [P, GRING, 2, N], F32R)

        w1_sb = sb("w1_sb", [P, T1, P])
        w1b_sb = sb("w1b_sb", [P, T1, P])
        w1x_sb = sb("w1x_sb", [P, 2, P])
        w1x_sum = sb("w1x_sum", [P, P])
        w1x_part = sb("w1x_part", [P, P], F32R)
        w1x_split = sb("w1x_split", [P, P], F32R)
        minus_sb = sb("minus_sb", [P, 2])
        w2_sb = sb("w2_sb", [P, T2, P])
        w2_part = sb("w2_part", [P, T2, P], F32R)
        w2_rest = sb("w2_rest", [P, T2, P], F32R)
        b1_sb, b2_sb = sb("b1_sb", [P, 1]), sb("b2_sb", [P, 1])
        wt1z1_sb, wt1z2_sb = sb("wt1z1_sb", [P, N1]), sb("wt1z2_sb", [P, N1])
        bt1_sb = sb("bt1_sb", [P, N1 // P])
        wt2_sb = sb("wt2_sb", [P, N1 // P, N2])
        bt2_sb = sb("bt2_sb", [P, N2 // P])
        wt3_sb = sb("wt3_sb", [P, N2 // P])
        z1_now, z2_now = sb("z1_now", [P, UB]), sb("z2_now", [P, UB])
        z1, z2 = sb("z1", [P, B]), sb("z2", [P, B])
        t1 = sb("t1", [P, N1 // P, B])
        t2 = sb("t2", [P, N2 // P, B])
        y_sb = sb("y_sb", [1, B])

        x1_ps = pb("x1_ps", [P, N])
        top2_ps = x1_ps[:, 0:N2 // P * B].rearrange("p (n b) -> p n b", b=B)
        x2_ps = pb("x2_ps", [P, N])
        head_ps = pb("head_ps", [P, N1 // P, B])
        y_ps = x2_ps[0:1, 0:B]

        s_ids, s_idx, s_idx_now = sem("s_ids"), sem("s_idx"), sem("s_idx_now")
        s_gather, s_store = [[sem(f"{n}{g}") for g in range(2)] for n in ("s_gather", "s_store")]
        s_store_first = sem("s_store_first")
        s_w1, s_w2, s_bias, s_head = sem("s_w1"), sem("s_w2"), sem("s_bias"), sem("s_head")
        s_ctx = sem("s_ctx")
        s_rep, s_x_sides = sem("s_rep"), sem("s_x_sides")
        s_roll = [sem(f"s_roll{t}") for t in range(T1)]
        s_hb = [sem(f"s_hb{j}") for j in range(B_ARR)]
        s_xa = [sem(f"s_xa{i}") for i in range(A_ARR)]
        s_w1_ready, s_w2_part, s_w2_rest = sem("s_w1_ready"), sem("s_w2_part"), sem("s_w2_rest")
        s_feat = sem("s_feat")
        s_part = sem("s_part")
        s_rest = sem("s_rest")
        s_tile = sem("s_tile")
        s_x1, s_x2 = sem("s_x1"), sem("s_x2")
        s_z1, s_z2 = sem("s_z1"), sem("s_z2")
        s_top1, s_t1, s_top2, s_t2 = sem("s_top1"), sem("s_t1"), sem("s_top2"), sem("s_t2")
        s_y_ps, s_y, s_out = sem("s_y_ps"), sem("s_y"), sem("s_out")

        def stored(pair, g):
            return (pair + g) * 32

        At = namedtuple("At", "tile step split")
        start = At(0, 0, 0)

        def at1(turn):
            return At(turn * PER + L1T, turn * STEPS + len(FORM1), turn * HI + 1)

        def at2(turn):
            return At(turn * PER + 2 * L1T, turn * STEPS + 2 * len(FORM1), turn * HI + 2)

        end = at1(U - 1)

        block = ctx.enter_context(nc.Block())

        @block.gpsimd
        def _(pool):
            def gather(u, g):
                nc.gpsimd.tensor_copy(idx_now[:, g], idx[:, bass.ds(u * NG, NG)]).then_inc(s_idx_now, 1)
                pool.wait_ge(s_idx_now, u + 1)
                pool.nop(nofuse=True)
                for n in range(NG):
                    pool.indirect_dma_start(
                        gathered[g][:, n * D:(n + 1) * D], None, table,
                        bass.IndirectOffsetOnAxis(ap=idx_now[:, g, n:n + 1], axis=0)).then_inc(s_gather[g], 16)

            def store(pair, g):
                pool.wait_ge(s_gather[g], (pair + 1) * (16 * NG))
                pool.nop(nofuse=True)
                for dst in store_dst:
                    pool.dma_start(dst[pair * 2 + g], gathered[g][:]).then_inc(s_store[g], 16)

            pool.wait_ge(s_ids, 32)
            nc.gpsimd.tensor_tensor(idx[:], ids_sb[:], offs_sb[:].to_broadcast([P, U * NG]), ALU.add).then_inc(s_idx, 1)
            pool.wait_ge(s_idx, 1)
            gather(0, 0)
            gather(1, 1)
            store(0, 1)
            pool.wait_ge(s_store_first, 32)
            gather(2, 0)
            pool.wait_ge(s_store[1], 32)
            gather(3, 1)
            for g in range(2):
                store(1, g)
            with pool.Fori(2, U // 2) as pair:
                for g in range(2):
                    pool.wait_ge(s_store[g], stored(pair - 1, g))
                    gather(pair * 2 + g, g)
                for g in range(2):
                    store(pair, g)

        @block.sync
        def _(sp):
            def load_layer1(unit, pair, g, before=None):
                if before is None:
                    sp.wait_ge(s_store_first, 32)
                    sp.dma_start(rep[:], rep_src[unit]).then_inc(s_rep, 16)
                else:
                    sp.wait_ge(s_store[g], stored(pair, g))
                    sp.nop(nofuse=True)
                for n, tiles in enumerate(FORM1):
                    if before is not None:
                        sp.wait_ge(s_feat, before.step + n + 1)
                        sp.nop(nofuse=True)
                        if n == len(FORM1) - 1:
                            sp.dma_start(rep[:], rep_src[unit]).then_inc(s_rep, 16)
                    if tiles == (FAR,):
                        for side in range(2):
                            for c in range(NC):
                                half = slice(c * XC * XF, (c + 1) * XC * XF)
                                sp.dma_start(x_sides[half, side], x_src[side][c][unit]).then_inc(s_x_sides, 16)
                    else:
                        for t in tiles:
                            sp.dma_start(roll[:, t, :], roll_src[t][unit]).then_inc(s_roll[t], 16)

            def load_b(unit, j):
                sp.dma_start(hb[:, j, :], b_src[j][unit]).then_inc(s_hb[j], 16)

            def load_a(i):
                src = x1[i:i + (HG - 1) * MG + 1:MG]
                sp.dma_start(xa[i][:], src.unsqueeze(1).to_broadcast([HG, MG, N])).then_inc(s_xa[i], 16)

            def turn(t, pair=None, g=0):
                if pair is not None:
                    load_layer1(t + 2, pair, g, at1(t))
                step = at2(t).step
                sp.wait_ge(s_x1, t + 2)
                sp.nop(nofuse=True)
                for i in range(A_ARR - 1):
                    sp.wait_ge(s_feat, step + B_ARR // 2 * (i + 1))
                    load_a(i)
                for j in range(B_ARR):
                    if j % 2 == 0:
                        sp.wait_ge(s_feat, step + (T2 - B_ARR + j) // 2 + 1)
                        sp.nop(nofuse=True)
                    load_b(t + 1, j)
                load_a(A_ARR - 1)

            sp.dma_start(ids_sb[:], ids).then_inc(s_ids, 16)
            sp.dma_start(offs_sb[:], offs).then_inc(s_ids, 16)
            sp.dma_start(w1_sb[:], w1a).then_inc(s_w1, 16)
            sp.dma_start(w1b_sb[:], w1b).then_inc(s_w1, 16)
            sp.dma_start(w1x_sb[:], w1x).then_inc(s_w1, 16)
            sp.dma_start(minus_sb[:], minus).then_inc(s_w1, 16)
            sp.dma_start(b1_sb[:], b1).then_inc(s_bias, 16)
            sp.dma_start(b2_sb[:], b2).then_inc(s_bias, 16)
            sp.dma_start(w2_sb[:], w2).then_inc(s_w2, 16)
            sp.wait_ge(s_gather[0], 16 * NG)
            for dst in store_dst:
                sp.dma_start(dst[0], gathered[0][:]).then_inc(s_store_first, 16)
            load_layer1(0, 0, 0)
            load_b(0, 0)
            load_b(0, 1)
            load_layer1(1, 0, 1, start)
            sp.wait_ge(s_x1, 1)
            load_a(0)
            load_b(0, 2)
            load_b(0, 3)
            for i in range(1, A_ARR):
                load_a(i)
            for dst, src in ((wt1z1_sb, wt1z1), (wt1z2_sb, wt1z2), (bt1_sb, bt1),
                             (wt2_sb, wt2), (bt2_sb, bt2), (wt3_sb, wt3)):
                sp.dma_start(dst[:], src).then_inc(s_head, 16)
            with sp.Fori(0, U // 2 - 1) as pair:
                for g in range(2):
                    turn(pair * 2 + g, pair + 1, g)
            turn(U - 2)
            sp.wait_ge(s_y, 1)
            sp.dma_start(out.rearrange("b o -> o b"), y_sb[:]).then_inc(s_out, 16)
            sp.wait_ge(s_out, 16)

        @block.vector
        def _(dve):
            def form_rest(dst, value, rounded, group):
                dve.wait_ge(s_part, group + 1)
                nc.vector.tensor_tensor(dst, value, rounded.bitcast(F32), ALU.subtract).then_inc(s_rest, 1)

            def split_rows(dst, value, rounded, column):
                return nc.vector.scalar_tensor_tensor(dst, rounded.bitcast(F32), minus_sb[:, column:column + 1],
                                                      value, ALU.mult, ALU.add)

            def layer1(unit, at, before=None):
                dve.wait_ge(s_rep, (unit + 1) * 16)
                for n, tiles in enumerate(FORM1):
                    if tiles == (FAR,):
                        dve.wait_ge(s_x_sides, (unit + 1) * (16 * 2 * NC))
                        out, a, b = feat_x[:], x_sides[:, 0], x_sides[:, 1]
                    else:
                        for t in tiles:
                            dve.wait_ge(s_roll[t], (unit + 1) * 16)
                        pair = slice(tiles[0], tiles[0] + 2)
                        out, a, b = feat1[:, pair, :], rep[:].unsqueeze(1).to_broadcast([P, 2, N]), roll[:, pair, :]
                    if before is not None and tiles == (FAR,):
                        dve.wait_ge(s_rest, before.split + 1)
                    elif before is not None:
                        dve.wait_ge(s_tile, before.tile + MULT1.index(tiles[-1]) + 1)
                    nc.vector.tensor_tensor(out, a, b, ALU.mult).then_inc(s_feat, 1)
                dve.wait_ge(s_feat, at.step + FORM1.index((FAR,)) + 1)
                dve.wait_ge(s_part, at.split + 1)
                if before is not None:
                    dve.wait_ge(s_tile, before.tile + MULT1.index(FAR) + 1)
                split_rows(split_x[:], feat_x[:], part_x[:], 1).then_inc(s_rest, 1)

            def layer2(unit, at, before=None):
                def rest_of(k):
                    q, n = SPLIT[k][0], len(SPLIT[k])
                    form_rest(rest[:, k % GRING, 0:n, :], feat2[:, q % RING:q % RING + n, :],
                              part[:, k % GRING, 0:n, :], at.split + k)

                for q in range(0, T2, 2):
                    i, j = divmod(q, B_ARR)
                    if j == 0:
                        dve.wait_ge(s_xa[i], (unit + 1) * 16)
                    if i == 0:
                        dve.wait_ge(s_hb[j], (unit + 1) * 16)
                        dve.wait_ge(s_hb[j + 1], (unit + 1) * 16)
                    if q >= RING:
                        dve.wait_ge(s_tile, at.tile + q + 1 - RING + 1)
                    elif before is not None:
                        dve.wait_ge(s_tile, before.tile + T2 + q + 1 - RING + 1)
                    slot = q % RING
                    nc.vector.tensor_tensor(feat2[:, slot:slot + 2, :], xa[i][:].unsqueeze(1).to_broadcast([P, 2, N]),
                                            hb[:, j:j + 2, :], ALU.mult).then_inc(s_feat, 1)
                    for k, after in enumerate(RESTS):
                        if after == q // 2:
                            rest_of(k)

            dve.wait_ge(s_w1, 64)
            nc.vector.tensor_tensor(w1_sb[:], w1_sb[:], w1b_sb[:], ALU.add).then_inc(s_w1_ready, 1)
            nc.vector.tensor_tensor(w1x_sum[:], w1x_sb[:, 0], w1x_sb[:, 1], ALU.add).then_inc(s_w1_ready, 1)
            dve.wait_ge(s_w1_ready, 2)
            nc.vector.tensor_copy(w1x_part[:], w1x_sum[:]).then_inc(s_w1_ready, 1)
            dve.wait_ge(s_w1_ready, 3)
            split_rows(w1x_split[:], w1x_sum[:], w1x_part[:], 0).then_inc(s_w1_ready, 1)
            dve.wait_ge(s_w2, 16)
            nc.vector.tensor_copy(w2_part[:], w2_sb[:]).then_inc(s_w2_part, 1)
            dve.wait_ge(s_w2_part, 1)
            nc.vector.tensor_tensor(w2_rest[:], w2_sb[:], w2_part[:].bitcast(F32), ALU.subtract).then_inc(s_w2_rest, 1)
            layer1(0, start)
            layer1(1, at1(0), start)
            layer2(0, at2(0))
            with dve.Fori(1, U - 1) as t:
                layer1(t + 1, at1(t), at1(t - 1))
                layer2(t, at2(t), at2(t - 1))
            layer2(U - 1, end, at2(U - 2))
            dve.wait_ge(s_y_ps, len(HEAD_PARTS))
            nc.vector.tensor_copy(y_sb[:], y_ps).then_inc(s_y, 1)

        @block.scalar
        def _(act):
            def round_x(at, before=None):
                act.wait_ge(s_feat, at.step + FORM1.index((FAR,)) + 1)
                if before is not None:
                    act.wait_ge(s_rest, before.split + 1)
                nc.scalar.activation(part_x[:], feat_x[:], ACT.Copy).then_inc(s_part, 1)

            def round_part(k, at, before=None):
                q, n = SPLIT[k][0], len(SPLIT[k])
                act.wait_ge(s_feat, at.step + q // 2 + 1)
                if k >= GRING:
                    act.wait_ge(s_tile, at.tile + SPLIT[k - GRING][-1] + 1)
                elif before is not None:
                    act.wait_ge(s_tile, before.tile + SPLIT[k - GRING][-1] + 1)
                nc.scalar.activation(part[:, k % GRING, 0:n, :], feat2[:, q % RING:q % RING + n, :],
                                     ACT.Copy).then_inc(s_part, 1)

            def relu_sums(samples, src, bias, dst, sums, done):
                for b in samples:
                    last = nc.scalar.activation(dst[:, b * D:(b + 1) * D], src[:, b * D:(b + 1) * D], ACT.Relu,
                                                bias=bias[:], accum_out=sums[:, b:b + 1])
                if UB - 1 in samples:
                    last.then_inc(done, 1)

            def keep(sums, kept, unit, read, done):
                act.wait_ge(read, unit + 1)
                nc.scalar.activation(kept[:, bass.ds(unit * UB, UB)], sums[:], ACT.Copy).then_inc(done, 1)

            def drain1(samples, unit, at, first=False):
                if 0 in samples:
                    act.wait_ge(s_tile, at.tile + L1T)
                    if not first:
                        act.wait_ge(s_z1, unit)
                        for i in range(A_ARR):
                            act.wait_ge(s_xa[i], unit * 16)
                relu_sums(samples, x2_ps if first else x1_ps, b1_sb, x1, z1_now, s_x1)

            def drain2(unit, at):
                act.wait_ge(s_tile, at.tile + T2)
                relu_sums(range(UB), x2_ps, b2_sb, x2_ps, z2_now, s_x2)
                keep(z2_now, z2, unit, s_x2, s_z2)

            def turn(t, before1, before2=None):
                round_x(at1(t), before1)
                if before2 is not None:
                    act.wait_ge(s_z1, t + 1)
                    drain2(t - 1, before2)
                drain1(range(UB // 2), t + 1, at1(t))
                round_part(0, at2(t), before2)
                drain1(range(UB // 2, UB), t + 1, at1(t))
                for k in range(1, len(SPLIT)):
                    round_part(k, at2(t), before2)
                keep(z1_now, z1, t + 1, s_x1, s_z1)

            def relu_top1(h):
                cols = HEAD_PARTS[h]
                for n in range(N1 // P):
                    act.wait_ge(s_top1, h * (N1 // P) + n + 1)
                    nc.scalar.activation(t1[:, n, cols], head_ps[:, n, cols], ACT.Relu,
                                         bias=bt1_sb[:, n:n + 1]).then_inc(s_t1, 1)

            def relu_top2(h):
                cols = HEAD_PARTS[h]
                for n in range(N2 // P):
                    act.wait_ge(s_top2, h * (N2 // P) + n + 1)
                    nc.scalar.activation(t2[:, n, cols], top2_ps[:, n, cols], ACT.Relu,
                                         bias=bt2_sb[:, n:n + 1]).then_inc(s_t2, 1)

            act.wait_ge(s_bias, 32)
            round_x(start)
            drain1(range(UB), 0, start, first=True)
            keep(z1_now, z1, 0, s_x1, s_z1)
            turn(0, start)
            with act.Fori(1, U - 1) as t:
                turn(t, at1(t - 1), at2(t - 1))
            act.wait_ge(s_z1, U)
            act.dma_start(z1[0:(CTX - 1) * MG + 1:MG], ctxT).then_inc(s_ctx, 16)
            drain2(U - 2, at2(U - 2))
            for k in range(len(SPLIT)):
                round_part(k, end, at2(U - 2))
            relu_top1(0)
            act.wait_ge(s_z2, U - 1)
            drain2(U - 1, end)
            relu_top2(0)
            relu_top1(1)
            relu_top2(1)

        @block.tensor
        def _(pe):
            def chunks(ps, w, x, start, stop):
                for c in range(NC):
                    last = nc.tensor.matmul(ps[:, c * BANK:(c + 1) * BANK], w, x[:, c * BANK:(c + 1) * BANK],
                                            start=start, stop=stop)
                return last

            def chunks_x(ps, start, stop):
                for c in range(NC):
                    held = slice(c * XC * XF, c * XC * XF + XK)
                    last = nc.tensor.matmul(ps[:, c * BANK:(c + 1) * BANK], w1x_split[held], split_x[held],
                                            start=start, stop=stop)
                return last

            def layer1(unit, at, ps):
                for n, t in enumerate(MULT1):
                    start, stop = n == 0, n == L1T - 1
                    if t == FAR:
                        pe.wait_ge(s_rest, at.split + 1)
                        chunks_x(ps, start, stop).then_inc(s_tile, 1)
                    else:
                        step, = [k for k, tiles in enumerate(FORM1) if t in tiles]
                        pe.wait_ge(s_feat, at.step + step + 1)
                        chunks(ps, w1_sb[:, t, :], feat1[:, t, :], start, stop).then_inc(s_tile, 1)

            def layer2(unit, at, fresh=False):
                if not fresh:
                    pe.wait_ge(s_x2, unit)
                whole = [q for q in range(T2) if not any(q in group for group in SPLIT)]
                for q in range(T2):
                    for k, group in enumerate(SPLIT):
                        if q != group[0]:
                            continue
                        pe.wait_ge(s_part, at.split + k + 1)
                        for n, g in enumerate(group):
                            chunks(x2_ps, w2_part[:, g, :], part[:, k % GRING, n, :], g == 0, False)
                            chunks(x2_ps, w2_rest[:, g, :], part[:, k % GRING, n, :], False, False)
                        pe.wait_ge(s_rest, at.split + k + 1)
                        for n, g in enumerate(group):
                            chunks(x2_ps, w2_part[:, g, :], rest[:, k % GRING, n, :],
                                   False, g == T2 - 1).then_inc(s_tile, 1)
                    if q in whole:
                        pe.wait_ge(s_feat, at.step + q // 2 + 1)
                        chunks(x2_ps, w2_sb[:, q, :], feat2[:, q % RING, :], q == 0, q == T2 - 1).then_inc(s_tile, 1)

            pe.wait_ge(s_w1_ready, 4)
            layer1(0, start, x2_ps)
            layer1(1, at1(0), x1_ps)
            pe.wait_ge(s_w2_rest, 1)
            pe.wait_ge(s_x1, 1)
            layer2(0, at2(0), fresh=True)
            with pe.Fori(1, U - 1) as t:
                pe.wait_ge(s_x1, t + 1)
                layer1(t + 1, at1(t), x1_ps)
                layer2(t, at2(t))

            def top1(h, units):
                cols = HEAD_PARTS[h]
                pe.wait_ge(s_z2, units)
                for n in range(N1 // P):
                    w = slice(n * P, (n + 1) * P)
                    nc.tensor.matmul(head_ps[:, n, cols], wt1z1_sb[:, w], z1[:, cols], start=True, stop=False)
                    nc.tensor.matmul(head_ps[:, n, cols], wt1z2_sb[:, w], z2[:, cols],
                                     start=False, stop=True).then_inc(s_top1, 1)

            def top2(h):
                cols = HEAD_PARTS[h]
                for n in range(N2 // P):
                    for k in range(N1 // P):
                        if n == 0:
                            pe.wait_ge(s_t1, h * (N1 // P) + k + 1)
                        last = nc.tensor.matmul(top2_ps[:, n, cols], wt2_sb[:, k, n * P:(n + 1) * P],
                                                t1[:, k, cols], start=k == 0, stop=k == N1 // P - 1)
                    last.then_inc(s_top2, 1)

            def top3(h):
                cols = HEAD_PARTS[h]
                for k in range(N2 // P):
                    pe.wait_ge(s_t2, h * (N2 // P) + k + 1)
                    last = nc.tensor.matmul(y_ps[:, cols], wt3_sb[:, k:k + 1], t2[:, k, cols],
                                            start=k == 0, stop=k == N2 // P - 1)
                last.then_inc(s_y_ps, 1)

            pe.wait_ge(s_head, 16 * HEAD_LOADS)
            pe.wait_ge(s_ctx, 16)
            top1(0, U - 2)
            layer2(U - 1, end)
            top2(0)
            top1(1, U)
            top3(0)
            top2(1)
            top3(1)


def kernel(**inputs):
    import numpy as np
    import concourse.bacc as bacc
    from concourse.bass_utils import run_bass_kernel_spmd

    x = {k: np.ascontiguousarray(v) for k, v in inputs.items()}
    tables = [x[f"tbl_{f}"] for f in range(F)]
    starts = np.cumsum([0] + [t.shape[0] for t in tables[:-1]]).astype(np.int32)
    f = np.arange(F)
    order = np.array([(r % MG % 4) * HG + r // MG + (64 if r % MG >= 4 else 0) for r in range(P)])
    w1 = x["L0_rec_W1"].reshape(P, F, F)[order]
    shift = np.arange(Q * T1).reshape(T1, Q)
    to = (f[None, None, :] + shift[:, :, None]) % F
    frm = np.broadcast_to(f, to.shape)
    w1a = w1[:, frm, to].transpose(2, 3, 1, 0).reshape(P, T1, P)
    w1b = w1[:, to, frm].transpose(2, 3, 1, 0).reshape(P, T1, P).copy()
    w1b[:F, 0] = 0.0
    low, high = f[:XF], f[XF:]
    w1x = np.stack([w1[:, low, high].T, w1[:, high, low].T], axis=1)
    copy = np.arange(P) // XF % XC
    w2 = x["L0_rec_W2"].reshape(P, A_ARR, HG, B_ARR, MG).transpose(2, 4, 1, 3, 0).reshape(P, T2, P)
    top1 = x["W_top1"]
    direct = order >= 64
    wt1z1 = np.zeros((P, N1), top1.dtype)
    wt1z1[direct] = top1[order[direct] - 64]
    wt1z1[0:(CTX - 1) * MG + 1:MG] = top1[64 + P:]
    arrays = {
        "ids": x["ids"].reshape(U, Q, NG, F).transpose(1, 3, 0, 2).reshape(P, U * NG),
        "offs": np.tile(starts, Q).reshape(P, 1),
        "table": np.concatenate(tables, axis=0),
        "w1a": w1a, "w1b": w1b, "w1x": np.tile(w1x, (NC * XC, 1, 1)),
        "minus": np.where(copy[:, None] == np.array([1, 2]), -1.0, 0.0).astype(np.float32),
        "b1": x["L0_rec_b1"][order].reshape(P, 1),
        "w2": w2, "b2": x["L0_rec_b2"].reshape(P, 1),
        "wt1z1": wt1z1, "wt1z2": top1[64:64 + P],
        "bt1": x["b_top1"].reshape(N1 // P, P).T,
        "wt2": x["W_top2"].reshape(N1 // P, P, N2).transpose(1, 0, 2),
        "bt2": x["b_top2"].reshape(N2 // P, P).T,
        "wt3": x["W_top3"].reshape(N2 // P, P).T,
        "ctxT": x["dense_ctx"].T,
    }
    nc = bacc.Bacc("TRN2", target_bir_lowering=False, num_devices=1)
    feed, aps = {}, []
    for name, a in arrays.items():
        a = np.ascontiguousarray(a)
        feed["in_" + name] = a
        aps.append(nc.dram_tensor("in_" + name, a.shape, mybir.dt.from_np(a.dtype), kind="ExternalInput").ap())
    aps.append(nc.dram_tensor("out_y", (B, 1), F32, kind="ExternalOutput").ap())
    build(nc, *aps)
    return run_bass_kernel_spmd(nc, [feed], core_ids=[0]).results[0]["out_y"]
```
